# Optimizing a Trainium2 kernel written in Bass

```python
import numpy as np
import jax
import jax.numpy as jnp

def _softmax(x, axis=-1):
    return jax.nn.softmax(x, axis=axis)

def _gelu(x):
    return jax.nn.gelu(x, approximate=True)

def _silu(x):
    return jax.nn.silu(x)

def _sigmoid(x):
    return jax.nn.sigmoid(x)

def _layernorm(x, axis=-1, eps=1e-05):
    m = jnp.mean(x, axis=axis, keepdims=True)
    v = jnp.var(x, axis=axis, keepdims=True)
    return (x - m) / jnp.sqrt(v + eps)

def _scatter_add(tgt, idx, src, axis=0):
    return tgt.at[idx].add(src)

def _segment_sum(src, seg, n):
    return jax.ops.segment_sum(src, seg, n)
kernel_name = 'mk_adaln_ffn_d1_seqx_r2_8be9c0'

def setup_inputs(seed: int=0):
    np.random.seed(seed)
    _w = jnp.asarray

    def _rec_inputs():
        import jax
        import jax.numpy as jnp
        _rk = jax.random.key(seed)
        x = -7.109e-05 + 0.9999 * jax.random.normal(jax.random.fold_in(_rk, 1), (64, 128, 2048), jnp.float32)
        _lenS = 128 - jax.random.randint(jax.random.fold_in(_rk, 7), (64,), 0, max(1, 128 // 4) + 1, jnp.int32)
        _lenS2 = 128 - jax.random.randint(jax.random.fold_in(_rk, 8), (64,), 0, max(1, 128 // 4) + 1, jnp.int32)
        itok_B_0_15 = jax.random.randint(jax.random.fold_in(_rk, 11), (64,), 0, 16, jnp.int32)
        return (x, itok_B_0_15)
    x, itok_B_0_15 = _rec_inputs()

    def _L0_cond_setup():
        import jax, jax.numpy as jnp
        import numpy as np
        B, C, T = (64, 128, 2048)
        S, D = (16, 128)
        key = jax.random.key(seed)
        k1, k2, k3 = jax.random.split(key, 3)
        x = jax.random.normal(k1, (B, C, T), dtype=jnp.float32)
        condition = jax.random.randint(k2, (B,), 0, S, dtype=jnp.int64)
        bound = float(np.sqrt(6.0 / C))
        weights = jax.random.uniform(k3, (S, C, D), dtype=jnp.float32, minval=-bound, maxval=bound)
        return {'x': x, 'condition': condition, 'weights': weights}
    _L0_cond_all = _L0_cond_setup()
    _L0_cond_in = {k: v for k, v in _L0_cond_all.items() if k in ('weights',)}
    del _L0_cond_all

    def _L0_ffn_setup():
        import jax, jax.numpy as jnp
        import numpy as np
        K_TOP = 8
        key = jax.random.key(seed)
        k1, k2, k3 = jax.random.split(key, 3)
        B, S, H, E = (4, 2048, 2048, 64)
        hidden_states = jax.random.normal(k1, (B, S, H), dtype=jnp.float32)
        router_weight = jax.random.normal(k2, (E, H), dtype=jnp.float32)
        router_bias = jnp.zeros((E,), dtype=jnp.float32)
        expert_bias = jax.random.normal(k3, (E, H), dtype=jnp.float32) * 0.1
        return {'hidden_states': hidden_states, 'router_weight': router_weight, 'router_bias': router_bias, 'expert_bias': expert_bias}
    _L0_ffn_all = _L0_ffn_setup()
    _L0_ffn_in = {k: v for k, v in _L0_ffn_all.items() if k in ('router_weight', 'router_bias', 'expert_bias')}
    del _L0_ffn_all
    return {'x': x, 'itok_B_0_15': itok_B_0_15, 'L0_cond_weights': _L0_cond_in['weights'], 'L0_ffn_router_weight': _L0_ffn_in['router_weight'], 'L0_ffn_router_bias': _L0_ffn_in['router_bias'], 'L0_ffn_expert_bias': _L0_ffn_in['expert_bias']}

def reference(x, itok_B_0_15, L0_cond_weights, L0_ffn_router_weight, L0_ffn_router_bias, L0_ffn_expert_bias):
    import jax
    import jax.numpy as jnp

    def _L0_cond_ref(x, condition, weights):
        import jax, jax.numpy as jnp
        import numpy as np
        B, C, T = (64, 128, 2048)
        S, D = (16, 128)
        W = weights[condition]
        return jnp.einsum('bct,bcd->bdt', x, W)

    def _L0_ffn_ref(hidden_states, router_weight, router_bias, expert_bias):
        import jax, jax.numpy as jnp
        import numpy as np
        K_TOP = 8
        B, S, H = hidden_states.shape
        E = router_weight.shape[0]
        T = B * S
        flat = hidden_states.reshape(T, H)
        logits = jnp.einsum('th,eh->te', flat, router_weight) + router_bias
        scores = jax.nn.softmax(logits, axis=-1)
        topk_w, topk_idx = jax.lax.top_k(scores, K_TOP)
        w_sum = topk_w.sum(axis=-1, keepdims=True)
        w_dense = jnp.zeros((T, E), dtype=scores.dtype).at[jnp.arange(T)[:, None], topk_idx].add(topk_w)
        bias_mix = jnp.einsum('te,eh->th', w_dense, expert_bias)
        out = flat * w_sum + bias_mix
        return out.reshape(B, S, H)
    x = x + _L0_ffn_ref(_L0_cond_ref(x, itok_B_0_15, L0_cond_weights), L0_ffn_router_weight, L0_ffn_router_bias, L0_ffn_expert_bias)
    return x

_drawn_inputs = setup_inputs


def setup_inputs(seed=0):
    import zlib

    import numpy as np

    out = dict(_drawn_inputs(seed))
    spreads = {'L0_ffn_router_bias': (0.0, 0.1)}
    factors = {}
    for name, (base, spread) in spreads.items():
        noise = np.random.default_rng([zlib.crc32(name.encode()), seed]).standard_normal(out[name].shape)
        drawn = base * np.exp(spread * noise) if base else spread * noise
        out[name] = jnp.asarray(drawn.astype(out[name].dtype))
    for name, factor in factors.items():
        out[name] = (out[name] * factor).astype(out[name].dtype)
    return out
```

```python
from contextlib import ExitStack

import concourse.bass as bass
from concourse import mybir

F32 = mybir.dt.float32
F32R = mybir.dt.float32r
I32 = mybir.dt.int32
ALU = mybir.AluOpType
ACT = mybir.ActivationFunctionType
AX = mybir.AxisListType

P = 128
PIECE = 512
LOWEST = -3.0e38
XRING = 4
UNROLL = 4


def adaln_router(nc, x, condition, weights, router_weight, router_bias, expert_bias, out):
    B, C, T = x.shape
    S, _, D = weights.shape
    E = router_weight.shape[0]
    PIECES = T // PIECE
    BLOCKS = PIECE // P
    TB = T // P
    HALF = T // 2
    PH = PIECES // 2
    LOOPS = B // UNROLL - 1
    assert C == P and D == P and E == 64 and B % UNROLL == 0 and PIECES == 4

    with ExitStack() as ctx:
        def sb(name, shape, dt=F32):
            return ctx.enter_context(nc.sbuf_tensor(name, shape, dt))

        def bank(name):
            return ctx.enter_context(nc.psum_tensor(name, [P, PIECE], F32))

        def sem(name):
            return ctx.enter_context(nc.semaphore(name))

        ident = sb("ident", [P, P])
        cond_sb = sb("cond_sb", [1, B], I32)
        bias_sb = sb("bias_sb", [P, E])
        router_sb = sb("router_sb", [E, T])
        router_hl = sb("router_hl", [P, TB, 2, E], F32R)
        expert_sb = sb("expert_sb", [P, T])
        expert_hl = sb("expert_hl", [P, T], F32R)
        w_all = sb("w_all", [P, S, D])
        w_all_hl = sb("w_all_hl", [P, 2, S, D], F32R)
        x_sb = sb("x_sb", [P, XRING, T])
        x_hi = sb("x_hi", [P, 2, T], F32R)
        x_lo = sb("x_lo", [P, 2, T], F32R)
        out_sb = sb("out_sb", [P, 2, T])
        w_sb = sb("w_sb", [P, 4, D])
        w_hl = sb("w_hl", [P, 4, 2, D], F32R)
        z_sb = sb("z_sb", [P, 2, E])
        kept_t_hi = sb("kept_t_hi", [P, 2, P], F32R)
        kept_t_lo = sb("kept_t_lo", [P, 2, P], F32R)
        w_sum = sb("w_sum", [P, 2, 1])
        xt_hi = sb("xt_hi", [P, 4, PIECE], F32R)
        xt_lo = sb("xt_lo", [P, 4, PIECE], F32R)
        logits = sb("logits", [P, E])
        rest = sb("rest", [P, E])
        top8 = sb("top8", [P, 8])
        neg_max = sb("neg_max", [P, 1])
        e_all = sb("e_all", [P, E])
        e_rest = sb("e_rest", [P, E])
        e_kept = sb("e_kept", [P, E])
        sums = sb("sums", [P, 2])
        inv_sums = sb("inv_sums", [P, 2])
        kept_twice = sb("kept_twice", [P, 2, E])

        xt_ps = [bank(f"xt_ps{i}") for i in range(2)]
        p_ps = [bank(f"p_ps{i}") for i in range(2)]
        z_ps = [bank(f"z_ps{i}") for i in range(2)]
        logits_ps = bank("logits_ps")
        kept_t_ps = bank("kept_t_ps")

        x_loaded = [sem(f"x_loaded{i}") for i in range(XRING)]
        out_stored = [sem(f"out_stored{i}") for i in range(2)]
        router_loaded = sem("router_loaded")
        w_loaded = sem("w_loaded")
        expert_loaded = sem("expert_loaded")
        bias_loaded = sem("bias_loaded")
        cond_loaded = sem("cond_loaded")
        ident_zero = sem("ident_zero")
        ident_ready = sem("ident_ready")
        router_in_ps = sem("router_in_ps")
        router_hi_ready = sem("router_hi_ready")
        router_ready = sem("router_ready")
        expert_hi_ready = sem("expert_hi_ready")
        expert_ready = sem("expert_ready")
        w_all_hi_ready = sem("w_all_hi_ready")
        w_all_ready = sem("w_all_ready")
        xt_in_ps = sem("xt_in_ps")
        xt_hi_ready = sem("xt_hi_ready")
        xt_lo_ready = sem("xt_lo_ready")
        routed = sem("routed")
        p_ready = sem("p_ready")
        finished = sem("finished")
        x_hi_ready = sem("x_hi_ready")
        x_lo_ready = sem("x_lo_ready")
        w_ready = sem("w_ready")
        z_ready = sem("z_ready")
        logits_in_ps = sem("logits_in_ps")
        logits_ready = sem("logits_ready")
        top8_ready = sem("top8_ready")
        rest_ready = sem("rest_ready")
        neg_max_ready = sem("neg_max_ready")
        exp_ready = sem("exp_ready")
        e_kept_ready = sem("e_kept_ready")
        inv_ready = sem("inv_ready")
        kept_ready = sem("kept_ready")
        w_sum_ready = sem("w_sum_ready")
        kept_t_in_ps = sem("kept_t_in_ps")
        kept_t_hi_ready = sem("kept_t_hi_ready")
        kept_t_ready = sem("kept_t_ready")

        def is_loop(m):
            return not isinstance(m, int)

        def wait(eng, s, value):
            if is_loop(value) or value > 0:
                eng.wait_ge(s, value)

        def steps(eng, step):
            for j in range(-UNROLL, 0):
                i = UNROLL + j
                step(0, j, True, i >= 1, i >= 2)
            with eng.Fori(0, LOOPS) as m:
                for j in range(UNROLL):
                    step(m, j, True, True, True)
            step(LOOPS, 0, False, True, True)
            step(LOOPS, 1, False, False, True)

        block = ctx.enter_context(nc.Block())

        @block.sync
        def _(sp):
            def load(m, o):
                wait(sp, finished, PIECES * (4 * m + o - XRING + 1))
                sp.dma_start(x_sb[:, o % XRING, :],
                             x[4 * m + o, :, :]).then_inc(x_loaded[o % XRING], 16)

            sp.dma_start(router_sb[:, :], router_weight).then_inc(router_loaded, 16)
            load(0, 0)
            sp.dma_start(cond_sb[:, :], condition).then_inc(cond_loaded, 16)
            sp.dma_start(w_all[:, :, :], weights.rearrange("s c d -> c s d")).then_inc(w_loaded, 16)
            load(0, 1)
            sp.dma_start(bias_sb[:, :], router_bias.to_broadcast([P, E])).then_inc(bias_loaded, 16)
            for r in range(2):
                sp.dma_start(expert_sb[r * E:(r + 1) * E, :], expert_bias).then_inc(expert_loaded, 16)
            load(0, 2)

            def store(m, o):
                for h in range(2):
                    sp.wait_ge(finished, PIECES * (4 * m + o) + PH * (h + 1))
                    sp.dma_start(out[4 * m + o, :, h * HALF:(h + 1) * HALF],
                                 out_sb[:, o % 2, h * HALF:(h + 1) * HALF]).then_inc(out_stored[o % 2], 16)

            load(0, 3)
            store(0, 0)
            with sp.Fori(0, LOOPS) as m:
                for i in range(UNROLL, 2 * UNROLL):
                    load(m, i)
                    store(m, i - 3)
            for o in range(1, UNROLL):
                store(LOOPS, o)
            for s in out_stored:
                sp.wait_ge(s, 16 * 2 * B // 2)

        @block.tensor
        def _(pe):
            def transposes(m, o, n):
                if n == 0:
                    pe.wait_ge(x_loaded[o % XRING], 16 * (m + o // XRING + 1))
                k = PIECES * (4 * m + o) + n
                wait(pe, xt_lo_ready, k - 1)
                for q in range(BLOCKS):
                    c0 = n * PIECE + q * P
                    last = pe.transpose(xt_ps[n % 2][:, q * P:(q + 1) * P],
                                        x_sb[:, o % XRING, c0:c0 + P], ident[:, :])
                last.then_inc(xt_in_ps, 1)

            def route(m, o, n):
                k = PIECES * (4 * m + o) + n
                if n == 0:
                    wait(pe, z_ready, 4 * m + o - 1)
                pe.wait_ge(xt_lo_ready, k + 1)
                z = z_ps[o % 2]
                for q in range(BLOCKS):
                    t = n * BLOCKS + q
                    pe.matmul(z[:, 0:2 * E], xt_hi[:, n, q * P:(q + 1) * P],
                              router_hl[:, t, :, :].rearrange("p a e -> p (a e)"),
                              start=(t == 0), stop=False)
                    last = pe.matmul(z[:, 0:E], xt_lo[:, n, q * P:(q + 1) * P],
                                     router_hl[:, t, 0, :], start=False, stop=(t == TB - 1))
                last.then_inc(routed, 1)

            def project(m, o, n):
                b = 4 * m + o
                if n % PH == 0:
                    pe.wait_ge(x_lo_ready, 2 * b + n // PH + 1)
                wait(pe, finished, PIECES * b + n - 1)
                acc = p_ps[n % 2][:, :]
                cols = slice(n * PIECE, (n + 1) * PIECE)
                pe.matmul(acc, w_hl[:, o % 4, 0, :], x_hi[:, o % 2, cols], start=True, stop=False)
                pe.matmul(acc, w_hl[:, o % 4, 0, :], x_lo[:, o % 2, cols], start=False, stop=False)
                pe.matmul(acc, w_hl[:, o % 4, 1, :], x_hi[:, o % 2, cols], start=False, stop=False)
                if n == 0:
                    pe.wait_ge(kept_t_ready, b + 1)
                pe.matmul(acc, kept_t_hi[:, o % 2, :], expert_hl[:, cols], start=False, stop=False)
                pe.matmul(acc, kept_t_lo[:, o % 2, :], expert_hl[:, cols],
                          start=False, stop=True).then_inc(p_ready, 1)

            def score(m, o):
                b = 4 * m + o
                pe.wait_ge(w_ready, 2 * (b + 1))
                wait(pe, logits_ready, b)
                pe.wait_ge(z_ready, b + 1)
                pe.matmul(logits_ps[:, 0:E], w_sb[:, o % 4, :], z_sb[:, o % 2, :],
                          start=True, stop=True).then_inc(logits_in_ps, 1)

            def turn_kept(m, o):
                b = 4 * m + o
                wait(pe, kept_t_ready, b)
                pe.wait_ge(kept_ready, b + 1)
                pe.transpose(kept_t_ps[:, 0:P], kept_twice[:, :, :].rearrange("p a e -> p (a e)"),
                             ident[:, :]).then_inc(kept_t_in_ps, 1)

            pe.wait_ge(ident_ready, 1)
            pe.wait_ge(router_loaded, 16)
            for t in range(TB):
                r = t % (TB // 2)
                last = pe.transpose(p_ps[t // (TB // 2)][:, r * E:(r + 1) * E],
                                    router_sb[:, t * P:(t + 1) * P], ident[0:E, 0:E])
            last.then_inc(router_in_ps, 1)

            def step(m, j, new, mid, old):
                i = UNROLL + j
                first = i == 0
                for n in range(PIECES):
                    if new:
                        transposes(m, i, n)
                    if mid and n == 1:
                        score(m, i - 1)
                    if old:
                        if i == 2 and n == 0:
                            pe.wait_ge(expert_ready, 1)
                        project(m, i - 2, n)
                    if mid and n == 3:
                        turn_kept(m, i - 1)
                    if n == 0 and mid:
                        route(m, i - 1, PIECES - 1)
                    if n > 0 and new:
                        if first and n == 1:
                            pe.wait_ge(router_ready, 2)
                        route(m, i, n - 1)

            steps(pe, step)

        @block.scalar
        def _(act):
            def xt_high(m, o, n):
                k = PIECES * (4 * m + o) + n
                act.wait_ge(xt_in_ps, k + 1)
                wait(act, routed, k - 3)
                act.copy(xt_hi[:, n, :], xt_ps[n % 2][:, :]).then_inc(xt_hi_ready, 1)

            def x_high(m, o, h):
                b = 4 * m + o
                act.wait_ge(x_loaded[o % XRING], 16 * (m + o // XRING + 1))
                wait(act, p_ready, PIECES * (b - 1))
                cols = slice(h * HALF, (h + 1) * HALF)
                act.copy(x_hi[:, o % 2, cols], x_sb[:, o % XRING, cols]).then_inc(x_hi_ready, 1)

            def exponentials(m, o):
                b = 4 * m + o
                wait(act, inv_ready, b)
                act.wait_ge(neg_max_ready, b + 1)
                act.activation(e_all[:, :], logits[:, :], ACT.Exp, bias=neg_max[:, 0:1],
                               accum_out=sums[:, 1:2]).then_inc(exp_ready, 1)
                act.wait_ge(rest_ready, b + 1)
                act.activation(e_rest[:, :], rest[:, :], ACT.Exp,
                               bias=neg_max[:, 0:1]).then_inc(exp_ready, 1)

            def kept_high(m, o):
                b = 4 * m + o
                wait(act, p_ready, PIECES * (b - 1))
                act.wait_ge(kept_t_in_ps, b + 1)
                act.copy(kept_t_hi[:, o % 2, :], kept_t_ps[:, 0:P]).then_inc(kept_t_hi_ready, 1)

            act.wait_ge(router_in_ps, 1)
            for g in range(2):
                act.copy(router_hl[:, g * TB // 2:(g + 1) * TB // 2, 0, :],
                         p_ps[g][:, :].rearrange("p (t e) -> p t e", e=E)).then_inc(router_hi_ready, 1)

            def split_constants():
                act.wait_ge(w_loaded, 16)
                act.copy(w_all_hl[:, 0, :, :], w_all[:, :, :]).then_inc(w_all_hi_ready, 1)
                act.wait_ge(expert_loaded, 32)
                act.copy(expert_hl[:, :], expert_sb[:, :]).then_inc(expert_hi_ready, 1)

            def step(m, j, new, mid, old):
                i = UNROLL + j
                for n in range(PIECES):
                    if new:
                        xt_high(m, i, n)
                    if mid and n < 2:
                        x_high(m, i - 1, n)
                    if mid and n == 2:
                        exponentials(m, i - 1)
                    if mid and n == 3:
                        kept_high(m, i - 1)
                if i == 0:
                    split_constants()

            steps(act, step)

        @block.vector
        def _(dve):
            def xt_low(m, o, n):
                k = PIECES * (4 * m + o) + n
                dve.wait_ge(xt_hi_ready, k + 1)
                dve.tensor_tensor(xt_lo[:, n, :], xt_ps[n % 2][:, :], xt_hi[:, n, :].bitcast(F32),
                                  ALU.subtract).then_inc(xt_lo_ready, 1)

            def z_sum(m, o):
                b = 4 * m + o
                dve.wait_ge(routed, PIECES * (b + 1))
                dve.tensor_reduce(z_sb[:, o % 2, :],
                                  z_ps[o % 2][:, 0:2 * E].rearrange("p (a e) -> p e a", a=2),
                                  AX.X, ALU.add).then_inc(z_ready, 1)

            def add_bias(m, o):
                b = 4 * m + o
                dve.wait_ge(logits_in_ps, b + 1)
                wait(dve, exp_ready, 2 * b)
                dve.tensor_tensor(logits[:, :], logits_ps[:, 0:E], bias_sb[:, :],
                                  ALU.add).then_inc(logits_ready, 1)

            def top(m, o):
                b = 4 * m + o
                dve.max(top8[:, :], logits[:, :]).then_inc(top8_ready, 1)
                dve.wait_ge(top8_ready, b + 1)
                dve.tensor_scalar(neg_max[:, :], top8[:, 0:1], -1.0, None,
                                  ALU.mult).then_inc(neg_max_ready, 1)
                dve.match_replace(rest[:, :], top8[:, :], logits[:, :], LOWEST).then_inc(rest_ready, 1)

            def keep(m, o):
                b = 4 * m + o
                dve.wait_ge(exp_ready, 2 * (b + 1))
                dve.scalar_tensor_tensor(e_kept[:, :], e_all[:, :], 1.0, e_rest[:, :], ALU.mult, ALU.subtract,
                                         accum_out=sums[:, 0:1]).then_inc(e_kept_ready, 1)
                dve.wait_ge(e_kept_ready, b + 1)
                dve.reciprocal(inv_sums[:, :], sums[:, :]).then_inc(inv_ready, 1)
                wait(dve, kept_t_in_ps, b)
                dve.wait_ge(inv_ready, b + 1)
                dve.tensor_scalar(kept_twice[:, :, :], e_kept[:, :].unsqueeze(1).to_broadcast([P, 2, E]),
                                  inv_sums[:, 0:1], None, ALU.mult).then_inc(kept_ready, 1)
                wait(dve, finished, PIECES * (b - 1))
                dve.tensor_tensor(w_sum[:, o % 2, :], sums[:, 0:1], inv_sums[:, 1:2],
                                  ALU.mult).then_inc(w_sum_ready, 1)

            def kept_low(m, o):
                dve.wait_ge(kept_t_hi_ready, 4 * m + o + 1)
                dve.tensor_tensor(kept_t_lo[:, o % 2, :], kept_t_ps[:, 0:P],
                                  kept_t_hi[:, o % 2, :].bitcast(F32), ALU.subtract).then_inc(kept_t_ready, 1)

            def finish(m, o, n):
                b = 4 * m + o
                cols = slice(n * PIECE, (n + 1) * PIECE)
                if n == 0:
                    dve.wait_ge(w_sum_ready, b + 1)
                    wait(dve, out_stored[o % 2], 32 * (2 * m + o // 2))
                dve.wait_ge(p_ready, PIECES * b + n + 1)
                dve.scalar_tensor_tensor(out_sb[:, o % 2, cols], p_ps[n % 2][:, :], w_sum[:, o % 2, :],
                                         x_sb[:, o % XRING, cols], ALU.mult, ALU.add).then_inc(finished, 1)

            for g in range(2):
                dve.wait_ge(router_hi_ready, g + 1)
                dve.tensor_tensor(router_hl[:, g * TB // 2:(g + 1) * TB // 2, 1, :],
                                  p_ps[g][:, :].rearrange("p (t e) -> p t e", e=E),
                                  router_hl[:, g * TB // 2:(g + 1) * TB // 2, 0, :].bitcast(F32),
                                  ALU.subtract).then_inc(router_ready, 1)

            def split_constants():
                dve.wait_ge(w_all_hi_ready, 1)
                dve.tensor_tensor(w_all_hl[:, 1, :, :], w_all[:, :, :],
                                  w_all_hl[:, 0, :, :].bitcast(F32), ALU.subtract).then_inc(w_all_ready, 1)
                dve.wait_ge(expert_hi_ready, 1)
                dve.tensor_tensor(expert_hl[E:2 * E, :], expert_sb[E:2 * E, :],
                                  expert_hl[E:2 * E, :].bitcast(F32), ALU.subtract).then_inc(expert_ready, 1)
                dve.wait_ge(bias_loaded, 16)

            def step(m, j, new, mid, old):
                i = UNROLL + j
                for n in range(PIECES):
                    if mid and n == 1:
                        z_sum(m, i - 1)
                    if new:
                        xt_low(m, i, n)
                    if mid and n == 1:
                        add_bias(m, i - 1)
                        dve.wait_ge(logits_ready, 4 * m + i)
                    if mid and n == 2:
                        keep(m, i - 1)
                    if old:
                        finish(m, i - 2, n)
                    if mid and n == 1:
                        top(m, i - 1)
                    if mid and n == 3:
                        kept_low(m, i - 1)
                if i == 0:
                    split_constants()

            steps(dve, step)

        @block.gpsimd
        def _(pool):
            pool.memset(ident[:, :], 0.0).then_inc(ident_zero, 1)
            pool.wait_ge(ident_zero, 1)
            pool.affine_select(out=ident[:, :], in_=ident[:, :], compare_op=ALU.not_equal, fill=1.0, base=0,
                               pattern=[[-1, P]], channel_multiplier=1).then_inc(ident_ready, 1)
            pool.wait_ge(cond_loaded, 16)
            pool.wait_ge(w_all_ready, 1)

            def pick_weights(m, o):
                b = 4 * m + o
                wait(pool, p_ready, PIECES * (b - 3))
                s = pool.value_load(cond_sb[0:1, bass.ds(b, 1)], min_val=0, max_val=S - 1)
                pool.tensor_copy(w_sb[:, o % 4, :],
                                 w_all[:, bass.ds(s, 1), :].rearrange("p a d -> p (a d)")).then_inc(w_ready, 1)
                pool.tensor_copy(w_hl[:, o % 4, :, :],
                                 w_all_hl[:, :, bass.ds(s, 1), :].rearrange("p h a d -> p h (a d)")
                                 .bitcast(F32)).then_inc(w_ready, 1)

            def x_low(m, o, h):
                b = 4 * m + o
                cols = slice(h * HALF, (h + 1) * HALF)
                pool.wait_ge(x_hi_ready, 2 * b + h + 1)
                pool.tensor_tensor(x_lo[:, o % 2, cols], x_sb[:, o % XRING, cols],
                                   x_hi[:, o % 2, cols].bitcast(F32), ALU.subtract).then_inc(x_lo_ready, 1)

            def step(m, j, new, mid, old):
                i = UNROLL + j
                if new:
                    pick_weights(m, i)
                if mid:
                    for h in range(2):
                        x_low(m, i - 1, h)

            steps(pool, step)


_INS = ["x", "itok_B_0_15", "L0_cond_weights", "L0_ffn_router_weight", "L0_ffn_router_bias", "L0_ffn_expert_bias"]


def kernel(**inputs):
    import numpy as np
    import concourse.bacc as bacc
    from concourse.bass_utils import run_bass_kernel_spmd

    nc = bacc.Bacc("TRN2", target_bir_lowering=False, num_devices=1)
    arrays, aps = {}, []
    for name in _INS:
        a = np.ascontiguousarray(inputs[name])
        if a.ndim == 1:
            a = a.reshape(1, -1)
        arrays[name] = a
        aps.append(nc.dram_tensor(name, a.shape, mybir.dt.from_np(a.dtype), kind="ExternalInput").ap())
    shape = inputs["x"].shape
    aps.append(nc.dram_tensor("out", shape, F32, kind="ExternalOutput").ap())
    adaln_router(nc, *aps)
    r = run_bass_kernel_spmd(nc, [arrays], core_ids=[0])
    return r.results[0]["out"]
```

```python
from contextlib import ExitStack

import concourse.bass as bass
from concourse import mybir

F32 = mybir.dt.float32
F32R = mybir.dt.float32r
I32 = mybir.dt.int32
ALU = mybir.AluOpType
ACT = mybir.ActivationFunctionType
AX = mybir.AxisListType

P = 128
PIECE = 512
LOWEST = -3.0e38
XRING = 8
UNROLL = 4


def adaln_router(nc, x, condition, weights, router_weight, router_bias, expert_bias, out):
    B, C, T = x.shape
    S, _, D = weights.shape
    E = router_weight.shape[0]
    PIECES = T // PIECE
    SLOTS = 2 * PIECES
    BLOCKS = PIECE // P
    TB = T // P
    HALF = T // 2
    PH = PIECES // 2
    LOOPS = B // 2 // UNROLL - 1
    assert C == P and D == P and E == 64 and B % (2 * UNROLL) == 0 and PIECES == 4

    with ExitStack() as ctx:
        def sb(name, shape, dt=F32):
            return ctx.enter_context(nc.sbuf_tensor(name, shape, dt))

        def bank(name):
            return ctx.enter_context(nc.psum_tensor(name, [P, PIECE], F32))

        def sem(name):
            return ctx.enter_context(nc.semaphore(name))

        ident = sb("ident", [P, P])
        ident_two = sb("ident_two", [P, E])
        cond_sb = sb("cond_sb", [1, B], I32)
        bias_sb = sb("bias_sb", [P, E])
        router_hl = sb("router_hl", [P, TB, 2, E], F32R)
        expert_hl = sb("expert_hl", [P, T], F32R)
        w_all_hl = sb("w_all_hl", [P, 2, S, D], F32R)
        x_sb = sb("x_sb", [P, XRING, T])
        x_hi = sb("x_hi", [P, 2, T], F32R)
        x_lo = sb("x_lo", [P, 2, T], F32R)
        out_sb = sb("out_sb", [P, 2, T])
        w_sb = sb("w_sb", [P, 4, D])
        w_hl = sb("w_hl", [P, 8, 2, D], F32R)
        xt_hi = sb("xt_hi", [P, 2, BLOCKS, 2, P], F32R)
        xt_lo = sb("xt_lo", [P, 2, BLOCKS, 2, P], F32R)
        kept_t_hi = sb("kept_t_hi", [P, 2, 2, P], F32R)
        kept_t_lo = sb("kept_t_lo", [P, 2, 2, P], F32R)
        w_sum = sb("w_sum", [P, 2, 2])
        zt_sb = sb("zt_sb", [P, 2, P])
        z_sb = sb("z_sb", [P, 2, E])
        logits = sb("logits", [P, 2, E])
        rest = sb("rest", [P, 2, E])
        top8 = sb("top8", [P, 2, 8])
        neg_max = sb("neg_max", [P, 2])
        e_all = sb("e_all", [P, 2, E])
        e_rest = sb("e_rest", [P, 2, E])
        e_kept = sb("e_kept", [P, 2, E])
        sums = sb("sums", [P, 2, 2])
        inv_sums = sb("inv_sums", [P, 2, 2])
        kept_twice = sb("kept_twice", [P, 2, 2, E])
        w_all = out_sb[:, 0, :].rearrange("p (s d) -> p s d", s=S)
        expert_sb = out_sb[:, 1, :]
        router_sb = x_sb[0:E, XRING - 1, :]

        xt_ps = [bank(f"xt_ps{i}") for i in range(2)]
        p_ps = [bank(f"p_ps{i}") for i in range(2)]
        zt_ps = bank("zt_ps")
        z_ps = bank("z_ps")
        logits_ps = bank("logits_ps")
        kept_t_ps = bank("kept_t_ps")

        x_loaded = [sem(f"x_loaded{i}") for i in range(XRING)]
        out_stored = [sem(f"out_stored{i}") for i in range(2)]
        router_loaded = sem("router_loaded")
        w_loaded = sem("w_loaded")
        expert_loaded = sem("expert_loaded")
        bias_loaded = sem("bias_loaded")
        cond_loaded = sem("cond_loaded")
        ident_zero = sem("ident_zero")
        ident_ready = sem("ident_ready")
        router_in_ps = sem("router_in_ps")
        router_hi_ready = sem("router_hi_ready")
        router_ready = sem("router_ready")
        expert_hi_ready = sem("expert_hi_ready")
        expert_ready = sem("expert_ready")
        w_all_hi_ready = sem("w_all_hi_ready")
        w_all_ready = sem("w_all_ready")
        xt_in_ps = sem("xt_in_ps")
        xt_hi_ready = sem("xt_hi_ready")
        xt_lo_ready = sem("xt_lo_ready")
        p_ready = sem("p_ready")
        finished = sem("finished")
        routed = sem("routed")
        x_hi_ready = sem("x_hi_ready")
        x_lo_ready = sem("x_lo_ready")
        w_hl_ready = sem("w_hl_ready")
        w_ready = sem("w_ready")
        zt_ready = sem("zt_ready")
        z_in_ps = sem("z_in_ps")
        z_ready = sem("z_ready")
        logits_in_ps = sem("logits_in_ps")
        logits_ready = sem("logits_ready")
        top8_ready = sem("top8_ready")
        rest_ready = sem("rest_ready")
        neg_max_ready = sem("neg_max_ready")
        exp_ready = sem("exp_ready")
        e_kept_ready = sem("e_kept_ready")
        inv_ready = sem("inv_ready")
        kept_ready = sem("kept_ready")
        w_sum_ready = sem("w_sum_ready")
        kept_t_in_ps = sem("kept_t_in_ps")
        kept_t_hi_ready = sem("kept_t_hi_ready")
        kept_t_ready = sem("kept_t_ready")

        def is_loop(m):
            return not isinstance(m, int)

        def wait(eng, s, value):
            if is_loop(value) or value > 0:
                eng.wait_ge(s, value)

        def steps(eng, step):
            for j in range(-UNROLL, 0):
                i = UNROLL + j
                step(0, j, True, i >= 1, i >= 2)
            with eng.Fori(0, LOOPS) as m:
                for j in range(UNROLL):
                    step(m, j, True, True, True)
            step(LOOPS, 0, False, True, True)
            step(LOOPS, 1, False, False, True)

        def loads(m, o, r):
            return 16 * (m + (2 * o + r) // XRING + 1)

        block = ctx.enter_context(nc.Block())

        @block.sync
        def _(sp):
            def load(m, o, r):
                b = 8 * m + 2 * o + r
                wait(sp, finished, PIECES * (b - XRING + 1))
                place = (2 * o + r) % XRING
                sp.dma_start(x_sb[:, place, :], x[b, :, :]).then_inc(x_loaded[place], 16)

            def store(m, o, r):
                b = 8 * m + 2 * o + r
                for h in range(2):
                    sp.wait_ge(finished, PIECES * b + PH * (h + 1))
                    sp.dma_start(out[b, :, h * HALF:(h + 1) * HALF],
                                 out_sb[:, r, h * HALF:(h + 1) * HALF]).then_inc(out_stored[r], 16)

            sp.dma_start(router_sb, router_weight).then_inc(router_loaded, 16)
            load(0, 0, 0)
            load(0, 0, 1)
            sp.dma_start(cond_sb[:, :], condition).then_inc(cond_loaded, 16)
            sp.dma_start(w_all, weights.rearrange("s c d -> c s d")).then_inc(w_loaded, 16)
            load(0, 1, 0)
            load(0, 1, 1)
            sp.dma_start(bias_sb[:, :], router_bias.to_broadcast([P, E])).then_inc(bias_loaded, 16)
            for r in range(2):
                sp.dma_start(expert_sb[r * E:(r + 1) * E, :], expert_bias).then_inc(expert_loaded, 16)
            load(0, 2, 0)
            load(0, 2, 1)
            sp.wait_ge(router_in_ps, 1)

            for r in range(2):
                load(0, 3, r)
                store(0, 0, r)
            with sp.Fori(0, LOOPS) as m:
                for i in range(UNROLL, 2 * UNROLL):
                    for r in range(2):
                        load(m, i, r)
                        store(m, i - 3, r)
            for o in range(1, UNROLL):
                for r in range(2):
                    store(LOOPS, o, r)
            for s in out_stored:
                sp.wait_ge(s, 16 * B)

        @block.tensor
        def _(pe):
            def transposes(m, o, v):
                r, n = v % 2, v // 2
                if n == 0:
                    pe.wait_ge(x_loaded[(2 * o + r) % XRING], loads(m, o, r))
                wait(pe, xt_lo_ready, SLOTS * (4 * m + o) + v - 1)
                for q in range(BLOCKS):
                    c0 = n * PIECE + q * P
                    last = pe.transpose(xt_ps[v % 2][:, q * P:(q + 1) * P],
                                        x_sb[:, (2 * o + r) % XRING, c0:c0 + P], ident[:, :])
                last.then_inc(xt_in_ps, 1)

            def route(m, o, n):
                i = 4 * m + o
                if n == 0:
                    wait(pe, zt_ready, i)
                pe.wait_ge(xt_lo_ready, SLOTS * i + 2 * n + 2)
                for q in range(BLOCKS):
                    t = n * BLOCKS + q
                    for xt in (xt_hi, xt_lo):
                        last = pe.matmul(zt_ps[:, 0:2 * P],
                                         router_hl[:, t, :, :].rearrange("p a e -> p (a e)"),
                                         xt[:, n % 2, q, :, :].rearrange("p r c -> p (r c)"),
                                         start=(t == 0 and xt is xt_hi),
                                         stop=(t == TB - 1 and xt is xt_lo))
                last.then_inc(routed, 1)

            def turn_z(m, o):
                i = 4 * m + o
                wait(pe, z_ready, i)
                pe.wait_ge(zt_ready, i + 1)
                for r in range(2):
                    last = pe.matmul(z_ps[:, r * E:(r + 1) * E], zt_sb[:, r, :], ident_two[:, :],
                                     start=True, stop=True)
                last.then_inc(z_in_ps, 1)

            def score(m, o):
                i = 4 * m + o
                pe.wait_ge(w_ready, 2 * i + 2)
                wait(pe, logits_ready, i)
                pe.wait_ge(z_ready, i + 1)
                for r in range(2):
                    last = pe.matmul(logits_ps[:, r * E:(r + 1) * E], w_sb[:, (2 * o + r) % 4, :],
                                     z_sb[:, r, :], start=True, stop=True)
                last.then_inc(logits_in_ps, 1)

            def turn_kept(m, o):
                i = 4 * m + o
                wait(pe, kept_t_ready, i)
                pe.wait_ge(kept_ready, 2 * i + 2)
                for r in range(2):
                    last = pe.transpose(kept_t_ps[:, r * P:(r + 1) * P],
                                        kept_twice[:, r, :, :].rearrange("p a e -> p (a e)"), ident[:, :])
                last.then_inc(kept_t_in_ps, 1)

            def project(m, o, v):
                r, n = v // PIECES, v % PIECES
                b = 8 * m + 2 * o + r
                if n % PH == 0:
                    pe.wait_ge(x_lo_ready, 2 * b + n // PH + 1)
                wait(pe, finished, PIECES * b + n - 1)
                acc = p_ps[n % 2][:, :]
                cols = slice(n * PIECE, (n + 1) * PIECE)
                w = w_hl[:, (2 * o + r) % 8, :, :]
                if n == 0:
                    pe.wait_ge(w_hl_ready, b + 1)
                pe.matmul(acc, w[:, 0, :], x_hi[:, r, cols], start=True, stop=False)
                pe.matmul(acc, w[:, 0, :], x_lo[:, r, cols], start=False, stop=False)
                pe.matmul(acc, w[:, 1, :], x_hi[:, r, cols], start=False, stop=False)
                if v == 0:
                    pe.wait_ge(kept_t_ready, 4 * m + o + 1)
                pe.matmul(acc, kept_t_hi[:, o % 2, r, :], expert_hl[:, cols], start=False, stop=False)
                pe.matmul(acc, kept_t_lo[:, o % 2, r, :], expert_hl[:, cols],
                          start=False, stop=True).then_inc(p_ready, 1)

            pe.wait_ge(ident_ready, 3)
            pe.wait_ge(router_loaded, 16)
            for t in range(TB):
                q = t % (TB // 2)
                last = pe.transpose(p_ps[t // (TB // 2)][:, q * E:(q + 1) * E],
                                    router_sb[:, t * P:(t + 1) * P], ident[0:E, 0:E])
            last.then_inc(router_in_ps, 1)

            def step(m, j, new, mid, old):
                i = UNROLL + j
                for v in range(SLOTS):
                    if new:
                        transposes(m, i, v)
                    if old:
                        if i == 2 and v == 0:
                            pe.wait_ge(expert_ready, 1)
                        project(m, i - 2, v)
                    if mid and v == 1:
                        turn_z(m, i - 1)
                    if mid and v == 2:
                        score(m, i - 1)
                    if mid and v == 6:
                        turn_kept(m, i - 1)
                    if mid and v == 0:
                        route(m, i - 1, PIECES - 1)
                    if new and v in (2, 4, 6):
                        if i == 0 and v == 2:
                            pe.wait_ge(router_ready, 2)
                        route(m, i, v // 2 - 1)

            steps(pe, step)

        @block.scalar
        def _(act):
            def xt_high(m, o, v):
                r, n = v % 2, v // 2
                i = 4 * m + o
                act.wait_ge(xt_in_ps, SLOTS * i + v + 1)
                wait(act, routed, PIECES * i + n - 1)
                act.copy(xt_hi[:, n % 2, :, r, :],
                         xt_ps[v % 2][:, :].rearrange("p (q c) -> p q c", c=P)).then_inc(xt_hi_ready, 1)

            def x_high(m, o, r, h):
                b = 8 * m + 2 * o + r
                act.wait_ge(x_loaded[(2 * o + r) % XRING], loads(m, o, r))
                wait(act, p_ready, PIECES * (b - 1))
                cols = slice(h * HALF, (h + 1) * HALF)
                act.copy(x_hi[:, r, cols], x_sb[:, (2 * o + r) % XRING, cols]).then_inc(x_hi_ready, 1)

            def zt_copy(m, o):
                i = 4 * m + o
                act.wait_ge(routed, PIECES * (i + 1))
                act.copy(zt_sb[:, :, :], zt_ps[:, 0:2 * P].rearrange("p (r c) -> p r c", r=2)).then_inc(zt_ready, 1)

            def z_copy(m, o):
                act.wait_ge(z_in_ps, 4 * m + o + 1)
                act.copy(z_sb[:, :, :], z_ps[:, 0:2 * E].rearrange("p (r e) -> p r e", r=2)).then_inc(z_ready, 1)

            def exponentials(m, o):
                i = 4 * m + o
                wait(act, inv_ready, i)
                act.wait_ge(neg_max_ready, i + 1)
                for r in range(2):
                    act.activation(e_all[:, r, :], logits[:, r, :], ACT.Exp, bias=neg_max[:, r:r + 1],
                                   accum_out=sums[:, 1, r:r + 1]).then_inc(exp_ready, 1)
                act.wait_ge(rest_ready, 2 * i + 2)
                for r in range(2):
                    act.activation(e_rest[:, r, :], rest[:, r, :], ACT.Exp,
                                   bias=neg_max[:, r:r + 1]).then_inc(exp_ready, 1)

            def kept_high(m, o):
                i = 4 * m + o
                wait(act, p_ready, SLOTS * (i - 1))
                act.wait_ge(kept_t_in_ps, i + 1)
                act.copy(kept_t_hi[:, o % 2, :, :],
                         kept_t_ps[:, 0:2 * P].rearrange("p (r c) -> p r c", r=2)).then_inc(kept_t_hi_ready, 1)

            act.wait_ge(router_in_ps, 1)
            for g in range(2):
                act.copy(router_hl[:, g * TB // 2:(g + 1) * TB // 2, 0, :],
                         p_ps[g][:, :].rearrange("p (t e) -> p t e", e=E)).then_inc(router_hi_ready, 1)

            def split_constants():
                act.wait_ge(w_loaded, 16)
                act.copy(w_all_hl[:, 0, :, :], w_all).then_inc(w_all_hi_ready, 1)
                act.wait_ge(expert_loaded, 32)
                act.copy(expert_hl[:, :], expert_sb).then_inc(expert_hi_ready, 1)

            def step(m, j, new, mid, old):
                i = UNROLL + j
                for v in range(SLOTS):
                    if mid and v == 1:
                        zt_copy(m, i - 1)
                    if mid and v == 2:
                        z_copy(m, i - 1)
                    if mid and v == 7:
                        kept_high(m, i - 1)
                    if new:
                        xt_high(m, i, v)
                    if old and v in (0, 2):
                        x_high(m, i - 2, 1, v // 2)
                    if mid and v in (5, 6):
                        x_high(m, i - 1, 0, v - 5)
                    if mid and v == 4:
                        exponentials(m, i - 1)
                if i == 0:
                    split_constants()

            steps(act, step)

        @block.vector
        def _(dve):
            def xt_low(m, o, v):
                r, n = v % 2, v // 2
                dve.wait_ge(xt_hi_ready, SLOTS * (4 * m + o) + v + 1)
                dve.tensor_tensor(xt_lo[:, n % 2, :, r, :], xt_ps[v % 2][:, :].rearrange("p (q c) -> p q c", c=P),
                                  xt_hi[:, n % 2, :, r, :].bitcast(F32), ALU.subtract).then_inc(xt_lo_ready, 1)

            def add_bias(m, o):
                i = 4 * m + o
                dve.wait_ge(logits_in_ps, i + 1)
                wait(dve, exp_ready, 4 * i)
                dve.tensor_tensor(logits[:, :, :], logits_ps[:, 0:2 * E].rearrange("p (r e) -> p r e", r=2),
                                  bias_sb[:, :].unsqueeze(1).to_broadcast([P, 2, E]),
                                  ALU.add).then_inc(logits_ready, 1)

            def top(m, o):
                for r in range(2):
                    dve.max(top8[:, r, :], logits[:, r, :]).then_inc(top8_ready, 1)
                dve.wait_ge(top8_ready, 2 * (4 * m + o) + 2)
                dve.tensor_scalar(neg_max[:, :], top8[:, :, 0], -1.0, None,
                                  ALU.mult).then_inc(neg_max_ready, 1)
                for r in range(2):
                    dve.match_replace(rest[:, r, :], top8[:, r, :], logits[:, r, :],
                                      LOWEST).then_inc(rest_ready, 1)

            def keep(m, o):
                i = 4 * m + o
                dve.wait_ge(exp_ready, 4 * i + 4)
                for r in range(2):
                    dve.scalar_tensor_tensor(e_kept[:, r, :], e_all[:, r, :], 1.0, e_rest[:, r, :],
                                             ALU.mult, ALU.subtract,
                                             accum_out=sums[:, 0, r:r + 1]).then_inc(e_kept_ready, 1)
                dve.wait_ge(e_kept_ready, 2 * i + 2)
                dve.reciprocal(inv_sums[:, :, :], sums[:, :, :]).then_inc(inv_ready, 1)
                wait(dve, kept_t_in_ps, i)
                dve.wait_ge(inv_ready, i + 1)
                for r in range(2):
                    dve.tensor_scalar(kept_twice[:, r, :, :],
                                      e_kept[:, r, :].unsqueeze(1).to_broadcast([P, 2, E]),
                                      inv_sums[:, 0, r:r + 1], None, ALU.mult).then_inc(kept_ready, 1)
                wait(dve, finished, SLOTS * (i - 1))
                dve.tensor_tensor(w_sum[:, o % 2, :], sums[:, 0, :], inv_sums[:, 1, :],
                                  ALU.mult).then_inc(w_sum_ready, 1)

            def kept_low(m, o):
                dve.wait_ge(kept_t_hi_ready, 4 * m + o + 1)
                dve.tensor_tensor(kept_t_lo[:, o % 2, :, :],
                                  kept_t_ps[:, 0:2 * P].rearrange("p (r c) -> p r c", r=2),
                                  kept_t_hi[:, o % 2, :, :].bitcast(F32), ALU.subtract).then_inc(kept_t_ready, 1)

            def finish(m, o, v):
                r, n = v // PIECES, v % PIECES
                cols = slice(n * PIECE, (n + 1) * PIECE)
                if v == 0:
                    dve.wait_ge(w_sum_ready, 4 * m + o + 1)
                if n == 0:
                    wait(dve, out_stored[r], 32 * (4 * m + o))
                dve.wait_ge(p_ready, SLOTS * (4 * m + o) + v + 1)
                dve.scalar_tensor_tensor(out_sb[:, r, cols], p_ps[n % 2][:, :], w_sum[:, o % 2, r:r + 1],
                                         x_sb[:, (2 * o + r) % XRING, cols],
                                         ALU.mult, ALU.add).then_inc(finished, 1)

            for g in range(2):
                dve.wait_ge(router_hi_ready, g + 1)
                dve.tensor_tensor(router_hl[:, g * TB // 2:(g + 1) * TB // 2, 1, :],
                                  p_ps[g][:, :].rearrange("p (t e) -> p t e", e=E),
                                  router_hl[:, g * TB // 2:(g + 1) * TB // 2, 0, :].bitcast(F32),
                                  ALU.subtract).then_inc(router_ready, 1)

            def split_constants():
                dve.wait_ge(w_all_hi_ready, 1)
                dve.tensor_tensor(w_all_hl[:, 1, :, :], w_all,
                                  w_all_hl[:, 0, :, :].bitcast(F32), ALU.subtract).then_inc(w_all_ready, 1)
                dve.wait_ge(expert_hi_ready, 1)
                dve.tensor_tensor(expert_hl[E:2 * E, :], expert_sb[E:2 * E, :],
                                  expert_hl[E:2 * E, :].bitcast(F32), ALU.subtract).then_inc(expert_ready, 1)
                dve.wait_ge(w_all_ready, 1)
                dve.wait_ge(expert_ready, 1)
                dve.wait_ge(bias_loaded, 16)

            def step(m, j, new, mid, old):
                i = UNROLL + j
                for v in range(SLOTS):
                    if new:
                        xt_low(m, i, v)
                    if mid and v == 3:
                        add_bias(m, i - 1)
                        dve.wait_ge(logits_ready, 4 * m + i)
                    if mid and v == 5:
                        keep(m, i - 1)
                    if old:
                        finish(m, i - 2, v)
                    if mid and v == 3:
                        top(m, i - 1)
                    if mid and v == 7:
                        kept_low(m, i - 1)
                if i == 0:
                    split_constants()

            steps(dve, step)

        @block.gpsimd
        def _(pool):
            for t in (ident, ident_two):
                pool.memset(t[:, :], 0.0).then_inc(ident_zero, 1)
            for n, (t, base) in enumerate(((ident, 0), (ident_two, 0), (ident_two, -E))):
                pool.wait_ge(ident_zero, 2)
                if n == 2:
                    pool.wait_ge(ident_ready, 2)
                pool.affine_select(out=t[:, :], in_=t[:, :], compare_op=ALU.not_equal, fill=1.0, base=base,
                                   pattern=[[-1, t.shape[1]]], channel_multiplier=1).then_inc(ident_ready, 1)
            pool.wait_ge(cond_loaded, 16)
            pool.wait_ge(w_all_ready, 1)

            def pick_weights(m, o, r):
                b = 8 * m + 2 * o + r
                w = w_hl[:, (2 * o + r) % 8, :, :]
                wait(pool, p_ready, PIECES * (b - 7))
                s = pool.value_load(cond_sb[0:1, bass.ds(b, 1)], min_val=0, max_val=S - 1)
                pool.tensor_copy(w, w_all_hl[:, :, bass.ds(s, 1), :].rearrange("p h a d -> p h (a d)")
                                 .bitcast(F32)).then_inc(w_hl_ready, 1)
                pool.wait_ge(w_hl_ready, b + 1)
                wait(pool, logits_in_ps, 4 * m + o - 1)
                pool.tensor_tensor(w_sb[:, (2 * o + r) % 4, :], w[:, 0, :].bitcast(F32),
                                   w[:, 1, :].bitcast(F32), ALU.add).then_inc(w_ready, 1)

            def x_low(m, o, r, h):
                b = 8 * m + 2 * o + r
                cols = slice(h * HALF, (h + 1) * HALF)
                pool.wait_ge(x_hi_ready, 2 * b + h + 1)
                pool.tensor_tensor(x_lo[:, r, cols], x_sb[:, (2 * o + r) % XRING, cols],
                                   x_hi[:, r, cols].bitcast(F32), ALU.subtract).then_inc(x_lo_ready, 1)

            def step(m, j, new, mid, old):
                i = UNROLL + j
                if old:
                    for h in range(2):
                        x_low(m, i - 2, 1, h)
                if new:
                    for r in range(2):
                        pick_weights(m, i, r)
                if mid:
                    for h in range(2):
                        x_low(m, i - 1, 0, h)

            steps(pool, step)


_INS = ["x", "itok_B_0_15", "L0_cond_weights", "L0_ffn_router_weight", "L0_ffn_router_bias", "L0_ffn_expert_bias"]


def kernel(**inputs):
    import numpy as np
    import concourse.bacc as bacc
    from concourse.bass_utils import run_bass_kernel_spmd

    nc = bacc.Bacc("TRN2", target_bir_lowering=False, num_devices=1)
    arrays, aps = {}, []
    for name in _INS:
        a = np.ascontiguousarray(inputs[name])
        if a.ndim == 1:
            a = a.reshape(1, -1)
        arrays[name] = a
        aps.append(nc.dram_tensor(name, a.shape, mybir.dt.from_np(a.dtype), kind="ExternalInput").ap())
    shape = inputs["x"].shape
    aps.append(nc.dram_tensor("out", shape, F32, kind="ExternalOutput").ap())
    adaln_router(nc, *aps)
    r = run_bass_kernel_spmd(nc, [arrays], core_ids=[0])
    return r.results[0]["out"]
```

```python
from contextlib import ExitStack

import concourse.bass as bass
from concourse import mybir

F32 = mybir.dt.float32
F32R = mybir.dt.float32r
I32 = mybir.dt.int32
ALU = mybir.AluOpType
ACT = mybir.ActivationFunctionType
AX = mybir.AxisListType

P = 128
PIECE = 512
LOWEST = -3.0e38
XRING = 8
UNROLL = 4


def adaln_router(nc, x, condition, weights, router_weight, router_bias, expert_bias, out):
    B, C, T = x.shape
    S, _, D = weights.shape
    E = router_weight.shape[0]
    PIECES = T // PIECE
    SLOTS = 2 * PIECES
    BLOCKS = PIECE // P
    TB = T // P
    HALF = T // 2
    PH = PIECES // 2
    LOOPS = B // 2 // UNROLL - 1
    assert C == P and D == P and E == 64 and B % (2 * UNROLL) == 0 and PIECES == 4

    with ExitStack() as ctx:
        def sb(name, shape, dt=F32):
            return ctx.enter_context(nc.sbuf_tensor(name, shape, dt))

        def bank(name):
            return ctx.enter_context(nc.psum_tensor(name, [P, PIECE], F32))

        def sem(name):
            return ctx.enter_context(nc.semaphore(name))

        ident = sb("ident", [P, P])
        cond_sb = sb("cond_sb", [1, B], I32)
        bias_sb = sb("bias_sb", [P, E])
        router_hl = sb("router_hl", [P, TB, 2, E], F32R)
        expert_hl = sb("expert_hl", [P, T], F32R)
        w_all_hl = sb("w_all_hl", [P, 2, S, D], F32R)
        x_sb = sb("x_sb", [P, XRING, T])
        x_hi = sb("x_hi", [P, 2, T], F32R)
        x_lo = sb("x_lo", [P, 2, T], F32R)
        out_sb = sb("out_sb", [P, 2, T])
        w_sb = sb("w_sb", [P, 4, D])
        w_hl = sb("w_hl", [P, 8, 2, D], F32R)
        xt_hi = sb("xt_hi", [P, 2, BLOCKS, 2, P], F32R)
        xt_lo = sb("xt_lo", [P, 2, BLOCKS, 2, P], F32R)
        kept_t_hi = sb("kept_t_hi", [P, 2, 2, P], F32R)
        kept_t_lo = sb("kept_t_lo", [P, 2, 2, P], F32R)
        w_sum = sb("w_sum", [P, 2, 2])
        zt_sb = sb("zt_sb", [P, 2, P])
        z_sb = sb("z_sb", [P, 2, E])
        logits = sb("logits", [P, 2, E])
        rest = sb("rest", [P, 2, E])
        top8 = sb("top8", [P, 2, 8])
        neg_max = sb("neg_max", [P, 2])
        e_all = sb("e_all", [P, 2, E])
        e_rest = sb("e_rest", [P, 2, E])
        e_kept = sb("e_kept", [P, 2, E])
        sums = sb("sums", [P, 2, 2])
        inv_sums = sb("inv_sums", [P, 2, 2])
        kept_twice = sb("kept_twice", [P, 2, 2, E])
        w_all = out_sb[:, 0, :].rearrange("p (s d) -> p s d", s=S)
        expert_sb = out_sb[:, 1, :]
        router_sb = x_sb[0:E, XRING - 1, :]

        xt_ps = [bank(f"xt_ps{i}") for i in range(4)]
        p_ps = [bank(f"p_ps{i}") for i in range(2)]
        zt_ps = bank("zt_ps")
        scores_ps = bank("scores_ps")
        z_ps = scores_ps[:, 0:4 * E]
        logits_ps = scores_ps[:, 4 * E:6 * E]
        kept_t_ps = scores_ps[:, 0:2 * P]

        x_loaded = [sem(f"x_loaded{i}") for i in range(XRING)]
        first_half_loaded = [sem(f"first_half_loaded{i}") for i in range(2)]
        out_stored = [sem(f"out_stored{i}") for i in range(2)]
        router_loaded = sem("router_loaded")
        w_loaded = sem("w_loaded")
        expert_loaded = sem("expert_loaded")
        bias_loaded = sem("bias_loaded")
        cond_loaded = sem("cond_loaded")
        ident_zero = sem("ident_zero")
        ident_ready = sem("ident_ready")
        router_in_ps = sem("router_in_ps")
        router_hi_ready = sem("router_hi_ready")
        router_ready = sem("router_ready")
        expert_hi_ready = sem("expert_hi_ready")
        expert_ready = sem("expert_ready")
        w_all_hi_ready = sem("w_all_hi_ready")
        w_all_ready = sem("w_all_ready")
        x_lo_ready = sem("x_lo_ready")
        xt_in_ps = sem("xt_in_ps")
        xt_hi_ready = sem("xt_hi_ready")
        xt_lo_ready = sem("xt_lo_ready")
        p_ready = sem("p_ready")
        finished = sem("finished")
        routed = sem("routed")
        x_hi_ready = sem("x_hi_ready")
        w_hl_ready = sem("w_hl_ready")
        w_ready = sem("w_ready")
        zt_ready = sem("zt_ready")
        z_in_ps = sem("z_in_ps")
        z_ready = sem("z_ready")
        logits_in_ps = sem("logits_in_ps")
        logits_ready = sem("logits_ready")
        top8_ready = sem("top8_ready")
        rest_ready = sem("rest_ready")
        neg_max_ready = sem("neg_max_ready")
        exp_ready = sem("exp_ready")
        e_kept_ready = sem("e_kept_ready")
        inv_ready = sem("inv_ready")
        kept_ready = sem("kept_ready")
        w_sum_ready = sem("w_sum_ready")
        kept_t_in_ps = sem("kept_t_in_ps")
        kept_t_hi_ready = sem("kept_t_hi_ready")
        kept_t_ready = sem("kept_t_ready")

        def is_loop(m):
            return not isinstance(m, int)

        def wait(eng, s, value):
            if is_loop(value) or value > 0:
                eng.wait_ge(s, value)

        def steps(eng, step):
            for j in range(-UNROLL, 0):
                i = UNROLL + j
                step(0, j, True, i >= 1, i >= 2)
            with eng.Fori(0, LOOPS) as m:
                for j in range(UNROLL):
                    step(m, j, True, True, True)
            step(LOOPS, 0, False, True, True)
            step(LOOPS, 1, False, False, True)

        def first(m, o):
            return not is_loop(m) and 4 * m + o == 0

        def loads(m, o, r):
            return 16 * (m + (2 * o + r) // XRING + 1)

        block = ctx.enter_context(nc.Block())

        @block.sync
        def _(sp):
            def load(m, o, r):
                b = 8 * m + 2 * o + r
                wait(sp, finished, PIECES * (b - XRING + 1))
                place = (2 * o + r) % XRING
                sp.dma_start(x_sb[:, place, :], x[b, :, :]).then_inc(x_loaded[place], 16)

            def store(m, o, r):
                b = 8 * m + 2 * o + r
                for h in range(2):
                    sp.wait_ge(finished, PIECES * b + PH * (h + 1))
                    sp.dma_start(out[b, :, h * HALF:(h + 1) * HALF],
                                 out_sb[:, r, h * HALF:(h + 1) * HALF]).then_inc(out_stored[r], 16)

            sp.dma_start(router_sb, router_weight).then_inc(router_loaded, 16)
            for h, landed in ((0, first_half_loaded), (1, x_loaded)):
                for r in range(2):
                    cols = slice(h * HALF, (h + 1) * HALF)
                    sp.dma_start(x_sb[:, r, cols], x[r, :, cols]).then_inc(landed[r], 16)
            sp.dma_start(cond_sb[:, :], condition).then_inc(cond_loaded, 16)
            sp.dma_start(w_all, weights.rearrange("s c d -> c s d")).then_inc(w_loaded, 16)
            load(0, 1, 0)
            load(0, 1, 1)
            sp.dma_start(bias_sb[:, :], router_bias.to_broadcast([P, E])).then_inc(bias_loaded, 16)
            for r in range(2):
                sp.dma_start(expert_sb[r * E:(r + 1) * E, :], expert_bias).then_inc(expert_loaded, 16)
            load(0, 2, 0)
            load(0, 2, 1)
            sp.wait_ge(router_in_ps, 1)

            for r in range(2):
                load(0, 3, r)
                store(0, 0, r)
            with sp.Fori(0, LOOPS) as m:
                for i in range(UNROLL, 2 * UNROLL):
                    for r in range(2):
                        load(m, i, r)
                        store(m, i - 3, r)
            for o in range(1, UNROLL):
                for r in range(2):
                    store(LOOPS, o, r)
            for s in out_stored:
                sp.wait_ge(s, 16 * B)

        @block.tensor
        def _(pe):
            def transposes(m, o, v):
                r, n = v % 2, v // 2
                if first(m, o) and n == 0:
                    pe.wait_ge(first_half_loaded[r], 16)
                if n == (PH if first(m, o) else 0):
                    pe.wait_ge(x_loaded[(2 * o + r) % XRING], loads(m, o, r))
                wait(pe, xt_lo_ready, SLOTS * (4 * m + o) + v - 3)
                for q in range(BLOCKS):
                    c0 = n * PIECE + q * P
                    last = pe.transpose(xt_ps[v % 4][:, q * P:(q + 1) * P],
                                        x_sb[:, (2 * o + r) % XRING, c0:c0 + P], ident[:, :])
                last.then_inc(xt_in_ps, 1)

            def route(m, o, n):
                i = 4 * m + o
                if n == 0:
                    wait(pe, zt_ready, i)
                pe.wait_ge(xt_lo_ready, SLOTS * i + 2 * n + 2)
                for q in range(BLOCKS):
                    t = n * BLOCKS + q
                    for xt in (xt_hi, xt_lo):
                        last = pe.matmul(zt_ps[:, 0:2 * P],
                                         router_hl[:, t, :, :].rearrange("p a e -> p (a e)"),
                                         xt[:, n % 2, q, :, :].rearrange("p r c -> p (r c)"),
                                         start=(t == 0 and xt is xt_hi),
                                         stop=(t == TB - 1 and xt is xt_lo))
                last.then_inc(routed, 1)

            def turn_z(m, o):
                i = 4 * m + o
                wait(pe, kept_t_ready, i)
                wait(pe, logits_ready, i)
                pe.wait_ge(zt_ready, i + 1)
                for r in range(2):
                    last = pe.transpose(z_ps[:, r * 2 * E:(r + 1) * 2 * E], zt_sb[:, r, :], ident[:, :])
                last.then_inc(z_in_ps, 1)

            def score(m, o):
                i = 4 * m + o
                pe.wait_ge(w_ready, 2 * i + 2)
                pe.wait_ge(z_ready, i + 1)
                for r in range(2):
                    last = pe.matmul(logits_ps[:, r * E:(r + 1) * E], w_sb[:, (2 * o + r) % 4, :],
                                     z_sb[:, r, :], start=True, stop=True)
                last.then_inc(logits_in_ps, 1)

            def turn_kept(m, o):
                i = 4 * m + o
                pe.wait_ge(kept_ready, 2 * i + 2)
                for r in range(2):
                    last = pe.transpose(kept_t_ps[:, r * P:(r + 1) * P],
                                        kept_twice[:, r, :, :].rearrange("p a e -> p (a e)"), ident[:, :])
                last.then_inc(kept_t_in_ps, 1)

            def project(m, o, v):
                r, n = v // PIECES, v % PIECES
                b = 8 * m + 2 * o + r
                pe.wait_ge(x_lo_ready, PIECES * b + n + 1)
                wait(pe, finished, PIECES * b + n - 1)
                acc = p_ps[n % 2][:, :]
                cols = slice(n * PIECE, (n + 1) * PIECE)
                w = w_hl[:, (2 * o + r) % 8, :, :]
                if n == 0:
                    pe.wait_ge(w_hl_ready, b + 1)
                pe.matmul(acc, w[:, 0, :], x_hi[:, r, cols], start=True, stop=False)
                pe.matmul(acc, w[:, 0, :], x_lo[:, r, cols], start=False, stop=False)
                pe.matmul(acc, w[:, 1, :], x_hi[:, r, cols], start=False, stop=False)
                if v == 0:
                    pe.wait_ge(kept_t_ready, 4 * m + o + 1)
                pe.matmul(acc, kept_t_hi[:, o % 2, r, :], expert_hl[:, cols], start=False, stop=False)
                pe.matmul(acc, kept_t_lo[:, o % 2, r, :], expert_hl[:, cols],
                          start=False, stop=True).then_inc(p_ready, 1)

            pe.wait_ge(ident_ready, 1)
            pe.wait_ge(router_loaded, 16)
            for t in range(TB):
                q = t % (TB // 2)
                last = pe.transpose(p_ps[t // (TB // 2)][:, q * E:(q + 1) * E],
                                    router_sb[:, t * P:(t + 1) * P], ident[0:E, 0:E])
            last.then_inc(router_in_ps, 1)

            def step(m, j, new, mid, old):
                i = UNROLL + j
                for v in range(SLOTS):
                    if new:
                        transposes(m, i, v)
                    if mid and v == 3:
                        score(m, i - 1)
                    if mid and v == 7:
                        turn_kept(m, i - 1)
                    if old:
                        if i == 2 and v == 0:
                            pe.wait_ge(expert_ready, 1)
                        project(m, i - 2, v)
                    if mid and v == 1:
                        turn_z(m, i - 1)
                    if mid and v == 0:
                        route(m, i - 1, PIECES - 1)
                    if new and v in ((2, 4, 6) if old else (3, 5, 7)):
                        if i == 0 and v == 3:
                            pe.wait_ge(router_ready, 2)
                        route(m, i, v // 2 - 1)

            steps(pe, step)

        @block.scalar
        def _(act):
            def xt_high(m, o, v):
                r, n = v % 2, v // 2
                i = 4 * m + o
                act.wait_ge(xt_in_ps, SLOTS * i + v + 1)
                wait(act, routed, PIECES * i + n - 1)
                act.copy(xt_hi[:, n % 2, :, r, :],
                         xt_ps[v % 4][:, :].rearrange("p (q c) -> p q c", c=P)).then_inc(xt_hi_ready, 1)

            def x_high(m, o, r, h):
                b = 8 * m + 2 * o + r
                act.wait_ge(x_loaded[(2 * o + r) % XRING], loads(m, o, r))
                wait(act, p_ready, PIECES * (b - 1))
                cols = slice(h * HALF, (h + 1) * HALF)
                act.copy(x_hi[:, r, cols], x_sb[:, (2 * o + r) % XRING, cols]).then_inc(x_hi_ready, 1)

            def zt_copy(m, o):
                i = 4 * m + o
                act.wait_ge(routed, PIECES * (i + 1))
                act.copy(zt_sb[:, :, :], zt_ps[:, 0:2 * P].rearrange("p (r c) -> p r c", r=2)).then_inc(zt_ready, 1)

            def exponentials(m, o):
                i = 4 * m + o
                wait(act, inv_ready, i)
                act.wait_ge(neg_max_ready, i + 1)
                for r in range(2):
                    act.activation(e_all[:, r, :], logits[:, r, :], ACT.Exp, bias=neg_max[:, r:r + 1],
                                   accum_out=sums[:, 1, r:r + 1]).then_inc(exp_ready, 1)
                act.wait_ge(rest_ready, 2 * i + 2)
                for r in range(2):
                    act.activation(e_rest[:, r, :], rest[:, r, :], ACT.Exp,
                                   bias=neg_max[:, r:r + 1]).then_inc(exp_ready, 1)

            def kept_high(m, o):
                i = 4 * m + o
                wait(act, p_ready, SLOTS * (i - 1))
                act.wait_ge(kept_t_in_ps, i + 1)
                act.copy(kept_t_hi[:, o % 2, :, :],
                         kept_t_ps.rearrange("p (r c) -> p r c", r=2)).then_inc(kept_t_hi_ready, 1)

            act.wait_ge(router_in_ps, 1)
            for g in range(2):
                act.copy(router_hl[:, g * TB // 2:(g + 1) * TB // 2, 0, :],
                         p_ps[g][:, :].rearrange("p (t e) -> p t e", e=E)).then_inc(router_hi_ready, 1)

            def step(m, j, new, mid, old):
                i = UNROLL + j
                for v in range(SLOTS):
                    if i == 0 and v == 7:
                        act.wait_ge(w_loaded, 16)
                        act.copy(w_all_hl[:, 0, :, :], w_all).then_inc(w_all_hi_ready, 1)
                    if i == 1 and v == 4:
                        act.wait_ge(expert_loaded, 32)
                        act.copy(expert_hl[:, :], expert_sb).then_inc(expert_hi_ready, 1)
                    if mid and v == 1:
                        zt_copy(m, i - 1)
                    if new:
                        xt_high(m, i, v)
                    if mid and v == 7:
                        kept_high(m, i - 1)
                    if old and v in (0, 2):
                        x_high(m, i - 2, 1, v // 2)
                    if mid and v in (5, 6):
                        x_high(m, i - 1, 0, v - 5)
                    if mid and v == 4:
                        exponentials(m, i - 1)

            steps(act, step)

        @block.vector
        def _(dve):
            def xt_low(m, o, v):
                r, n = v % 2, v // 2
                dve.wait_ge(xt_hi_ready, SLOTS * (4 * m + o) + v + 1)
                dve.tensor_tensor(xt_lo[:, n % 2, :, r, :], xt_ps[v % 4][:, :].rearrange("p (q c) -> p q c", c=P),
                                  xt_hi[:, n % 2, :, r, :].bitcast(F32), ALU.subtract).then_inc(xt_lo_ready, 1)

            def z_sum(m, o):
                dve.wait_ge(z_in_ps, 4 * m + o + 1)
                dve.tensor_reduce(z_sb[:, :, :], z_ps.rearrange("p (r a e) -> p r e a", r=2, a=2),
                                  AX.X, ALU.add).then_inc(z_ready, 1)

            def add_bias(m, o):
                i = 4 * m + o
                dve.wait_ge(logits_in_ps, i + 1)
                wait(dve, exp_ready, 4 * i)
                dve.tensor_tensor(logits[:, :, :], logits_ps.rearrange("p (r e) -> p r e", r=2),
                                  bias_sb[:, :].unsqueeze(1).to_broadcast([P, 2, E]),
                                  ALU.add).then_inc(logits_ready, 1)

            def top(m, o):
                for r in range(2):
                    dve.max(top8[:, r, :], logits[:, r, :]).then_inc(top8_ready, 1)
                dve.wait_ge(top8_ready, 2 * (4 * m + o) + 2)
                dve.tensor_scalar(neg_max[:, :], top8[:, :, 0], -1.0, None,
                                  ALU.mult).then_inc(neg_max_ready, 1)
                for r in range(2):
                    dve.match_replace(rest[:, r, :], top8[:, r, :], logits[:, r, :],
                                      LOWEST).then_inc(rest_ready, 1)

            def keep(m, o):
                i = 4 * m + o
                dve.wait_ge(exp_ready, 4 * i + 4)
                for r in range(2):
                    dve.scalar_tensor_tensor(e_kept[:, r, :], e_all[:, r, :], 1.0, e_rest[:, r, :],
                                             ALU.mult, ALU.subtract,
                                             accum_out=sums[:, 0, r:r + 1]).then_inc(e_kept_ready, 1)
                dve.wait_ge(e_kept_ready, 2 * i + 2)
                dve.reciprocal(inv_sums[:, :, :], sums[:, :, :]).then_inc(inv_ready, 1)

            def norm(m, o):
                i = 4 * m + o
                wait(dve, kept_t_in_ps, i)
                dve.wait_ge(inv_ready, i + 1)
                for r in range(2):
                    dve.tensor_scalar(kept_twice[:, r, :, :],
                                      e_kept[:, r, :].unsqueeze(1).to_broadcast([P, 2, E]),
                                      inv_sums[:, 0, r:r + 1], None, ALU.mult).then_inc(kept_ready, 1)
                wait(dve, finished, SLOTS * (i - 1))
                dve.tensor_tensor(w_sum[:, o % 2, :], sums[:, 0, :], inv_sums[:, 1, :],
                                  ALU.mult).then_inc(w_sum_ready, 1)

            def kept_low(m, o):
                dve.wait_ge(kept_t_hi_ready, 4 * m + o + 1)
                dve.tensor_tensor(kept_t_lo[:, o % 2, :, :],
                                  kept_t_ps.rearrange("p (r c) -> p r c", r=2),
                                  kept_t_hi[:, o % 2, :, :].bitcast(F32), ALU.subtract).then_inc(kept_t_ready, 1)

            def finish(m, o, v):
                r, n = v // PIECES, v % PIECES
                cols = slice(n * PIECE, (n + 1) * PIECE)
                if v == 0:
                    dve.wait_ge(w_sum_ready, 4 * m + o + 1)
                if n == 0:
                    wait(dve, out_stored[r], 32 * (4 * m + o))
                dve.wait_ge(p_ready, SLOTS * (4 * m + o) + v + 1)
                dve.scalar_tensor_tensor(out_sb[:, r, cols], p_ps[n % 2][:, :], w_sum[:, o % 2, r:r + 1],
                                         x_sb[:, (2 * o + r) % XRING, cols],
                                         ALU.mult, ALU.add).then_inc(finished, 1)

            for g in range(2):
                dve.wait_ge(router_hi_ready, g + 1)
                dve.tensor_tensor(router_hl[:, g * TB // 2:(g + 1) * TB // 2, 1, :],
                                  p_ps[g][:, :].rearrange("p (t e) -> p t e", e=E),
                                  router_hl[:, g * TB // 2:(g + 1) * TB // 2, 0, :].bitcast(F32),
                                  ALU.subtract).then_inc(router_ready, 1)

            def step(m, j, new, mid, old):
                i = UNROLL + j
                for v in range(SLOTS):
                    if i == 1 and v == 0:
                        dve.wait_ge(w_all_hi_ready, 1)
                        dve.tensor_tensor(w_all_hl[:, 1, :, :], w_all, w_all_hl[:, 0, :, :].bitcast(F32),
                                          ALU.subtract).then_inc(w_all_ready, 1)
                    if i == 1 and v == 5:
                        dve.wait_ge(expert_hi_ready, 1)
                        dve.tensor_tensor(expert_hl[E:2 * E, :], expert_sb[E:2 * E, :],
                                          expert_hl[E:2 * E, :].bitcast(F32),
                                          ALU.subtract).then_inc(expert_ready, 1)
                    if new:
                        xt_low(m, i, v)
                    if mid and v == 7:
                        kept_low(m, i - 1)
                    if mid and v == 2:
                        z_sum(m, i - 1)
                    if mid and v == 3:
                        if i == 1:
                            dve.wait_ge(bias_loaded, 16)
                        add_bias(m, i - 1)
                        dve.wait_ge(logits_ready, 4 * m + i)
                    if mid and v == 5:
                        keep(m, i - 1)
                    if old:
                        if i == 2 and v == 0:
                            dve.wait_ge(w_all_ready, 1)
                            dve.wait_ge(expert_ready, 1)
                        finish(m, i - 2, v)
                    if mid and v == 3:
                        top(m, i - 1)
                    if mid and v == 5:
                        norm(m, i - 1)

            steps(dve, step)

        @block.gpsimd
        def _(pool):
            pool.memset(ident[:, :], 0.0).then_inc(ident_zero, 1)
            pool.wait_ge(ident_zero, 1)
            pool.affine_select(out=ident[:, :], in_=ident[:, :], compare_op=ALU.not_equal, fill=1.0, base=0,
                               pattern=[[-1, P]], channel_multiplier=1).then_inc(ident_ready, 1)
            pool.wait_ge(cond_loaded, 16)
            pool.wait_ge(w_all_ready, 1)

            def pick_weights(m, o, r):
                b = 8 * m + 2 * o + r
                w = w_hl[:, (2 * o + r) % 8, :, :]
                wait(pool, p_ready, PIECES * (b - 7))
                s = pool.value_load(cond_sb[0:1, bass.ds(b, 1)], min_val=0, max_val=S - 1)
                pool.tensor_copy(w, w_all_hl[:, :, bass.ds(s, 1), :].rearrange("p h a d -> p h (a d)")
                                 .bitcast(F32)).then_inc(w_hl_ready, 1)
                pool.wait_ge(w_hl_ready, b + 1)
                wait(pool, logits_in_ps, 4 * m + o - 1)
                pool.tensor_tensor(w_sb[:, (2 * o + r) % 4, :], w[:, 0, :].bitcast(F32),
                                   w[:, 1, :].bitcast(F32), ALU.add).then_inc(w_ready, 1)

            def x_low(m, o, r):
                b = 8 * m + 2 * o + r
                for n in range(PIECES):
                    cols = slice(n * PIECE, (n + 1) * PIECE)
                    if n % PH == 0:
                        pool.wait_ge(x_hi_ready, 2 * b + n // PH + 1)
                    pool.tensor_tensor(x_lo[:, r, cols], x_sb[:, (2 * o + r) % XRING, cols],
                                       x_hi[:, r, cols].bitcast(F32), ALU.subtract).then_inc(x_lo_ready, 1)

            def step(m, j, new, mid, old):
                i = UNROLL + j
                if old:
                    x_low(m, i - 2, 1)
                if new:
                    for r in range(2):
                        pick_weights(m, i, r)
                if mid:
                    x_low(m, i - 1, 0)

            steps(pool, step)


_INS = ["x", "itok_B_0_15", "L0_cond_weights", "L0_ffn_router_weight", "L0_ffn_router_bias", "L0_ffn_expert_bias"]


def kernel(**inputs):
    import numpy as np
    import concourse.bacc as bacc
    from concourse.bass_utils import run_bass_kernel_spmd

    nc = bacc.Bacc("TRN2", target_bir_lowering=False, num_devices=1)
    arrays, aps = {}, []
    for name in _INS:
        a = np.ascontiguousarray(inputs[name])
        if a.ndim == 1:
            a = a.reshape(1, -1)
        arrays[name] = a
        aps.append(nc.dram_tensor(name, a.shape, mybir.dt.from_np(a.dtype), kind="ExternalInput").ap())
    shape = inputs["x"].shape
    aps.append(nc.dram_tensor("out", shape, F32, kind="ExternalOutput").ap())
    adaln_router(nc, *aps)
    r = run_bass_kernel_spmd(nc, [arrays], core_ids=[0])
    return r.results[0]["out"]
```
